# Optimizing a Trainium2 kernel written in Bass

```python
import numpy as np
import jax
import jax.numpy as jnp

def _softmax(x, axis=-1):
    return jax.nn.softmax(x, axis=axis)

def _gelu(x):
    return jax.nn.gelu(x, approximate=True)

def _silu(x):
    return jax.nn.silu(x)

def _sigmoid(x):
    return jax.nn.sigmoid(x)

def _layernorm(x, axis=-1, eps=1e-05):
    m = jnp.mean(x, axis=axis, keepdims=True)
    v = jnp.var(x, axis=axis, keepdims=True)
    return (x - m) / jnp.sqrt(v + eps)

def _scatter_add(tgt, idx, src, axis=0):
    return tgt.at[idx].add(src)

def _segment_sum(src, seg, n):
    return jax.ops.segment_sum(src, seg, n)
kernel_name = 'mk_adj_preln_d1_adj_r2_42ec4a'

def setup_inputs(seed: int=0):
    np.random.seed(seed)
    _w = jnp.asarray

    def _rec_inputs():
        import jax
        import jax.numpy as jnp
        _gk = jax.random.key(seed)
        x = -0.001003 + 1 * jax.random.normal(jax.random.fold_in(_gk, 1), (6144, 128), jnp.float32)
        _a = jax.random.bernoulli(jax.random.fold_in(_gk, 2), 0.000651042, (6144, 6144))
        adj = _a.astype(jnp.int32)
        return (x, adj)
    x, adj = _rec_inputs()

    def _L0_gnn_setup():
        import jax, jax.numpy as jnp
        import numpy as np
        M = 6144
        N = 6144
        D = 128
        TEMPERATURE = 0.07
        NEG_PAD = jnp.float32(-2 ** 32 + 1)
        key = jax.random.key(seed)
        k1, k2, k3, k4 = jax.random.split(key, 4)
        xx_anchor = jax.random.normal(k1, (M, D), dtype=jnp.float32)
        inp = jax.random.normal(k2, (N, D), dtype=jnp.float32)
        adj = (jax.random.uniform(k3, (M, N)) < 0.002).astype(jnp.int32)
        limit = jnp.sqrt(6.0 / (D + D)).astype(jnp.float32)
        weight = jax.random.uniform(k4, (D, D), minval=-limit, maxval=limit, dtype=jnp.float32)
        return {'xx_anchor': xx_anchor, 'input': inp, 'adj': adj, 'weight': weight}
    _L0_gnn_all = _L0_gnn_setup()
    _L0_gnn_in = {k: v for k, v in _L0_gnn_all.items() if k in ('input', 'weight')}
    del _L0_gnn_all
    return {'x': x, 'adj': adj, 'L0_gnn_input': _L0_gnn_in['input'], 'L0_gnn_weight': _L0_gnn_in['weight']}

def reference(x, adj, L0_gnn_input, L0_gnn_weight):
    import jax
    import jax.numpy as jnp

    def _L0_gnn_ref(xx_anchor, input, adj, weight):
        import jax, jax.numpy as jnp
        import numpy as np
        M = 6144
        N = 6144
        D = 128
        TEMPERATURE = 0.07
        NEG_PAD = jnp.float32(-2 ** 32 + 1)
        anchor_adj = jnp.einsum('md,de,ne->mn', xx_anchor, weight, input)
        scores = jnp.where(adj > 0, anchor_adj, NEG_PAD)
        atten = jax.nn.softmax(scores / TEMPERATURE, axis=1)
        return atten @ input
    h = jnp.maximum(_layernorm(x, axis=-1), 0.0)
    x = x + _L0_gnn_ref(h, L0_gnn_input, adj, L0_gnn_weight)
    return x

_drawn_inputs = setup_inputs


def setup_inputs(seed=0):
    import zlib

    import numpy as np

    out = dict(_drawn_inputs(seed))
    spreads = {}
    factors = {}
    for name, (base, spread) in spreads.items():
        noise = np.random.default_rng([zlib.crc32(name.encode()), seed]).standard_normal(out[name].shape)
        drawn = base * np.exp(spread * noise) if base else spread * noise
        out[name] = jnp.asarray(drawn.astype(out[name].dtype))
    for name, factor in factors.items():
        out[name] = (out[name] * factor).astype(out[name].dtype)
    return out
```

```python
import concourse.bass as bass
from concourse import mybir
from contextlib import ExitStack


def gnn_masked_attention_kernel(
    nc: bass.Bass,
    x: bass.AP,
    adj: bass.AP,
    nodes: bass.AP,
    weight: bass.AP,
    out: bass.AP,
):
    fp32 = mybir.dt.float32
    fp32r = mybir.dt.float32r
    bf16 = mybir.dt.bfloat16
    int32 = mybir.dt.int32
    ALU = mybir.AluOpType
    ACT = mybir.ActivationFunctionType
    AX = mybir.AxisListType

    M, D = x.shape
    N = nodes.shape[0]
    P = 128
    TILES = M // P
    BLOCKS = N // P
    TURN = 512
    TURNS = N // TURN
    PER_TURN = TURN // P
    SCORE = 1024
    SCORES = N // SCORE
    CONV = 2048
    CONVS = N // CONV
    PER_CONV = CONV // SCORE
    PER_EXP = SCORE // TURN
    EPS = 1e-5
    SMALL = 2.0 ** -64
    EXP_SCALE = 2.0 ** 64 / 0.07
    LOWEST = -3.0e38
    S_AT = {0: 1, 2: 2, 3: 3, 5: 4, 6: 5}
    H_AT = 4
    E_AT = {8: 0, 9: 1, 10: 2, 11: 3}
    E_LATE = {0: 4, 1: 5}

    adj_v = adj.rearrange("(t p) n -> t p n", p=P)
    x_v = x.rearrange("(t p) d -> t p d", p=P)
    out_v = out.rearrange("(t p) d -> t p d", p=P)
    nodes_v = nodes.rearrange("(b p) d -> p b d", p=P)

    ctx = ExitStack()
    with ctx:
        def sb(name, shape, dt):
            return ctx.enter_context(nc.sbuf_tensor(name, shape, dt))

        def pb(name, shape, dt):
            return ctx.enter_context(nc.psum_tensor(name, shape, dt))

        def sem(name):
            return ctx.enter_context(nc.semaphore(name))

        yT_hi = sb("yT_hi", [P, N], fp32r)
        yT_lo = sb("yT_lo", [P, N], fp32r)
        v = sb("v", [P, BLOCKS, 2, D], fp32r)
        probs = sb("probs", [P, 2, N], fp32)
        adj_i = sb("adj_i", [P, CONVS, CONV], int32)
        absent = sb("absent", [P, CONVS, CONV], bf16)
        pT_hi = sb("pT_hi", [P, 2, TURN], fp32r)
        pT_lo = sb("pT_lo", [P, 2, TURN], fp32r)
        hT = sb("hT", [P, 2, P], fp32)
        hT_hi = sb("hT_hi", [P, 2, P], fp32r)
        hT_lo = sb("hT_lo", [P, 2, P], fp32r)
        h = sb("h", [P, 2, D], fp32)
        x_ln = sb("x_ln", [P, 2, D], fp32)
        x_res = sb("x_res", [P, 2, D], fp32)
        fin_a = sb("fin_a", [P, 2, D], fp32)
        fin = sb("fin", [P, 2, D], fp32)
        ident = sb("ident", [P, P], fp32)
        w = sb("w", [P, D], fp32)
        wT = sb("wT", [P, D], fp32)
        minus_half = sb("minus_half", [P, 1], fp32)
        stats = sb("stats", [P, 2, 6], fp32)
        mean_var = sb("mean_var", [P, 2, 2], fp32)
        var_eps = sb("var_eps", [P, 2, 1], fp32)
        rstd = sb("rstd", [P, 2, 1], fp32)
        chunk_max = sb("chunk_max", [P, 2, SCORES], fp32)
        row_max = sb("row_max", [P, 2, 1], fp32)
        neg_max = sb("neg_max", [P, 2, 1], fp32)
        chunk_sum = sb("chunk_sum", [P, 2, SCORES], fp32)
        row_sum = sb("row_sum", [P, 2, 1], fp32)
        inv_sum = sb("inv_sum", [P, 2, 1], fp32)
        nodes_raw = probs[:, 0, :].rearrange("p (b d) -> p b d", d=D)
        nodesT = probs[:, 1, 0:2 * TURN].rearrange("p (s n) -> p s n", s=2)

        ps_s = [pb(f"ps_s{i}", [P, SCORE], fp32) for i in range(2)]
        ps_t = [pb(f"ps_t{i}", [P, TURN], fp32) for i in range(2)]
        ps_o = [pb(f"ps_o{i}", [P, 512], fp32) for i in range(2)]

        w_in = sem("w_in")
        nodes_in = sem("nodes_in")
        x_ln_in = [sem(f"x_ln_in{i}") for i in range(2)]
        x_res_in = [sem(f"x_res_in{i}") for i in range(2)]
        adj_in = [sem(f"adj_in{i}") for i in range(CONVS)]
        stored = [sem(f"stored{i}") for i in range(2)]
        ident_zero = sem("ident_zero")
        ident_done = sem("ident_done")
        half_done = sem("half_done")
        absent_done = sem("absent_done")
        stats_done = sem("stats_done")
        aggr_done = sem("aggr_done")
        var_done = sem("var_done")
        rstd_done = sem("rstd_done")
        h_done = sem("h_done")
        h_turned = sem("h_turned")
        hT_done = sem("hT_done")
        hT_hi_done = sem("hT_hi_done")
        hT_lo_done = sem("hT_lo_done")
        turned = sem("turned")
        turn_freed = sem("turn_freed")
        y_made = sem("y_made")
        y_hi_done = sem("y_hi_done")
        y_lo_done = sem("y_lo_done")
        v_hi_done = sem("v_hi_done")
        v_lo_done = sem("v_lo_done")
        scores_made = sem("scores_made")
        masked = sem("masked")
        max_done = sem("max_done")
        neg_max_done = sem("neg_max_done")
        exp_done = sem("exp_done")
        pT_hi_done = sem("pT_hi_done")
        pv_done = sem("pv_done")
        sum_done = sem("sum_done")
        inv_done = sem("inv_done")
        fin_a_done = sem("fin_a_done")
        fin_done = sem("fin_done")

        pool_waited = sem("pool_waited")
        dve_waited = sem("dve_waited")

        SETUP_TURNS = 1 + TURNS

        def turn_no(t, k):
            return t * TURNS + (SETUP_TURNS + k)

        def turn_bank(k):
            return (SETUP_TURNS + k) % 2

        def steps(eng, step):
            for t in range(3):
                step(t, t // 2, t % 2, t)
            with eng.Fori(0, (TILES - 6) // 2) as i:
                step(i * 2 + 3, i + 1, 1, None)
                step(i * 2 + 4, i + 2, 0, None)
            for t in range(TILES - 3, TILES):
                step(t, t // 2, t % 2, t)

        def has(at, ahead):
            return at is None or at + ahead < TILES

        block = ctx.enter_context(nc.Block())

        @block.sync
        def _(sp):
            sp.dma_start(w[:, :], weight).then_inc(w_in, 16)
            sp.dma_start(nodes_raw, nodes_v).then_inc(nodes_in, 16)
            for t in range(2):
                sp.dma_start(x_ln[:, t, :], x_v[t]).then_inc(x_ln_in[t], 16)
            for c in range(CONVS):
                sp.dma_start(adj_i[:, c, :], adj_v[0][:, c * CONV:(c + 1) * CONV]).then_inc(adj_in[c], 16)
            sp.dma_start(x_res[:, 0, :], x_v[0]).then_inc(x_res_in[0], 16)
            sp.wait_ge(h_done, 1)
            sp.dma_start(x_ln[:, 0, :], x_v[2]).then_inc(x_ln_in[0], 16)
            for c in range(CONVS):
                sp.wait_ge(absent_done, c + 1)
                sp.dma_start(adj_i[:, c, :], adj_v[1][:, c * CONV:(c + 1) * CONV]).then_inc(adj_in[c], 16)

            def step(t, half, par, at):
                if has(at, 3):
                    sp.wait_ge(h_done, t + 2)
                    s = (par + 3) % 2
                    sp.dma_start(x_ln[:, s, :], x_v[t + 3]).then_inc(x_ln_in[s], 16)
                if has(at, 2):
                    for c in range(CONVS):
                        sp.wait_ge(absent_done, t * CONVS + (CONVS + c + 1))
                        sp.dma_start(adj_i[:, c, :], adj_v[t + 2][:, c * CONV:(c + 1) * CONV])\
                            .then_inc(adj_in[c], 16)
                if has(at, 1):
                    if at != 0:
                        sp.wait_ge(fin_done, t)
                    s = (par + 1) % 2
                    sp.dma_start(x_res[:, s, :], x_v[t + 1]).then_inc(x_res_in[s], 16)

            steps(sp, step)

        @block.gpsimd
        def _(pool):
            nc.gpsimd.memset(ident[:, :], 0.0).then_inc(ident_zero, 1)
            nc.gpsimd.memset(minus_half[:, :], -0.5).then_inc(half_done, 1)
            pool.wait_ge(ident_zero, 1)
            nc.gpsimd.affine_select(out=ident[:, :], in_=ident[:, :], compare_op=ALU.not_equal, fill=1.0,
                                    base=0, pattern=[[-1, P]], channel_multiplier=1).then_inc(ident_done, 1)
            pool.wait_ge(half_done, 1)

            def make_h(u, s, free):
                pool.wait_ge(aggr_done, u + 1)
                pool.sem_inc(pool_waited, 1)
                nc.gpsimd.tensor_scalar(var_eps[:, s, :], mean_var[:, s, 1:2], EPS, None, ALU.add)\
                    .then_inc(var_done, 1)
                pool.wait_ge(var_done, u + 1)
                nc.gpsimd.tensor_tensor(rstd[:, s, :], var_eps[:, s, :], minus_half[:, :], ALU.pow)\
                    .then_inc(rstd_done, 1)
                pool.wait_ge(rstd_done, u + 1)
                if free:
                    pool.wait_ge(h_turned, u - 1)
                pool.sem_inc(pool_waited, 1)
                nc.gpsimd.tensor_scalar(h[:, s, :], x_ln[:, s, :], mean_var[:, s, 0:1], rstd[:, s, :],
                                        ALU.subtract, ALU.mult).then_inc(h_done, 1)

            def convert(u, c, free):
                pool.wait_ge(adj_in[c], u * 16 + 16)
                if free:
                    pool.wait_ge(masked, u * SCORES + (PER_CONV * (c + 1) - SCORES))
                pool.sem_inc(pool_waited, 1)
                nc.gpsimd.tensor_scalar(absent[:, c, :], adj_i[:, c, :], 0.0, -1.0, ALU.is_gt, ALU.add)\
                    .then_inc(absent_done, 1)

            make_h(0, 0, False)
            make_h(1, 1, False)
            for c in range(CONVS):
                convert(0, c, False)

            def step(t, half, par, at):
                if has(at, 1):
                    convert(t + 1, 0, True)
                if has(at, 2):
                    make_h(t + 2, par, True)
                if has(at, 1):
                    for c in range(1, CONVS):
                        convert(t + 1, c, True)

            steps(pool, step)

        @block.scalar
        def _(act):
            act.wait_ge(nodes_in, 16)
            for k in range(TURNS):
                b = k * PER_TURN
                nc.scalar.activation(v[:, b:b + PER_TURN, 0, :], nodes_raw[:, b:b + PER_TURN, :], ACT.Copy)\
                    .then_inc(v_hi_done, 1)
                act.wait_ge(y_made, k + 1)
                nc.scalar.activation(yT_hi[:, k * TURN:(k + 1) * TURN], ps_s[k % 2][:, 0:TURN], ACT.Copy)\
                    .then_inc(y_hi_done, 1)

            def split_h(u, s, free):
                act.wait_ge(hT_done, u + 1)
                if free:
                    act.wait_ge(scores_made, u * SCORES - SCORES)
                nc.scalar.activation(hT_hi[:, s, :], hT[:, s, :], ACT.Copy).then_inc(hT_hi_done, 1)

            def exp(u, s, c):
                act.wait_ge(neg_max_done, u + 1)
                part = probs[:, s, c * SCORE:(c + 1) * SCORE]
                nc.scalar.activation(part, part, ACT.Exp, bias=neg_max[:, s, :], scale=EXP_SCALE,
                                     accum_out=chunk_sum[:, s, c:c + 1]).then_inc(exp_done, 1)

            split_h(0, 0, False)
            split_h(1, 1, False)
            for c in E_AT.values():
                exp(0, 0, c)

            def step(t, half, par, at):
                for k in range(TURNS):
                    act.wait_ge(turned, turn_no(t, k) + 1)
                    if k >= 2 or at != 0:
                        act.wait_ge(pv_done, t * TURNS + (k - 1))
                    nc.scalar.activation(pT_hi[:, k % 2, :], ps_t[turn_bank(k)][:, :], ACT.Copy)\
                        .then_inc(pT_hi_done, 1)
                    if k in E_LATE:
                        exp(t, par, E_LATE[k])
                    if k == H_AT + 1 and has(at, 2):
                        split_h(t + 2, par, True)
                    if k == H_AT + 2 and at != 0:
                        act.wait_ge(fin_done, t)
                        act.dma_start(out_v[t - 1], fin[:, 1 - par, :]).then_inc(stored[1 - par], 16)
                    if k in E_AT and has(at, 1):
                        exp(t + 1, 1 - par, E_AT[k])

            steps(act, step)
            act.wait_ge(fin_done, TILES)
            last = (TILES - 1) % 2
            act.dma_start(out_v[TILES - 1], fin[:, last, :]).then_inc(stored[last], 16)
            for s in range(2):
                act.wait_ge(stored[s], 16 * (TILES // 2))

        @block.vector
        def _(dve):
            def x_stats(u, half, s):
                dve.wait_ge(x_ln_in[s], half * 16 + 16)
                nc.vector.bn_stats(stats[:, s, :], x_ln[:, s, :]).then_inc(stats_done, 1)
                dve.wait_ge(stats_done, u + 1)
                dve.sem_inc(dve_waited, 1)
                nc.vector.bn_aggr(mean_var[:, s, :], stats[:, s, :]).then_inc(aggr_done, 1)

            def relu_h(u, s):
                dve.wait_ge(h_turned, u + 1)
                nc.vector.tensor_scalar(hT[:, s, :], ps_o[1 - s][:, 0:P], 0.0, SMALL, ALU.max, ALU.mult)\
                    .then_inc(hT_done, 1)

            def lo_h(u, s):
                dve.wait_ge(hT_hi_done, u + 1)
                nc.vector.tensor_tensor(hT_lo[:, s, :], hT[:, s, :], hT_hi[:, s, :].bitcast(fp32), ALU.subtract)\
                    .then_inc(hT_lo_done, 1)

            def mask(u, s, j):
                dve.wait_ge(absent_done, u * CONVS + (j // PER_CONV + 1))
                dve.wait_ge(scores_made, u * SCORES + (j + 1))
                dve.sem_inc(dve_waited, 1)
                c, part = j // PER_CONV, j % PER_CONV
                nc.vector.tensor_tensor_reduce(
                    out=probs[:, s, j * SCORE:(j + 1) * SCORE],
                    in0=absent[:, c, part * SCORE:(part + 1) * SCORE], in1=ps_s[j % 2][:, :],
                    scale=1.0, scalar=LOWEST, op0=ALU.add, op1=ALU.max,
                    accum_out=chunk_max[:, s, j:j + 1]).then_inc(masked, 1)

            def find_max(u, s):
                dve.wait_ge(masked, u * SCORES + SCORES)
                nc.vector.tensor_reduce(row_max[:, s, :], chunk_max[:, s, :], AX.X, ALU.max).then_inc(max_done, 1)
                dve.wait_ge(max_done, u + 1)
                nc.vector.tensor_scalar(neg_max[:, s, :], row_max[:, s, :], -EXP_SCALE, None, ALU.mult)\
                    .then_inc(neg_max_done, 1)

            def finish(u, half, s, free):
                dve.wait_ge(exp_done, u * SCORES + SCORES)
                nc.vector.reduce_sum(row_sum[:, s, :], chunk_sum[:, s, :], AX.X).then_inc(sum_done, 1)
                dve.wait_ge(sum_done, u + 1)
                nc.vector.reciprocal(inv_sum[:, s, :], row_sum[:, s, :]).then_inc(inv_done, 1)
                dve.wait_ge(inv_done, u + 1)
                dve.wait_ge(x_res_in[s], half * 16 + 16)
                dve.wait_ge(pv_done, u * TURNS + TURNS)
                nc.vector.scalar_tensor_tensor(out=fin_a[:, s, :], in0=ps_o[s][:, 0:D], scalar=inv_sum[:, s, :],
                                               in1=x_res[:, s, :], op0=ALU.mult, op1=ALU.add)\
                    .then_inc(fin_a_done, 1)
                dve.wait_ge(fin_a_done, u + 1)
                if free:
                    dve.wait_ge(stored[s], half * 16)
                nc.vector.scalar_tensor_tensor(out=fin[:, s, :], in0=ps_o[s][:, D:2 * D], scalar=inv_sum[:, s, :],
                                               in1=fin_a[:, s, :], op0=ALU.mult, op1=ALU.add)\
                    .then_inc(fin_done, 1)

            dve.wait_ge(turned, 1)
            nc.vector.tensor_copy(wT[:, :], ps_t[0][:, 0:D]).then_inc(turn_freed, 1)
            x_stats(0, 0, 0)
            x_stats(1, 0, 1)

            def y_lo(k):
                dve.wait_ge(y_hi_done, k + 1)
                cols = slice(k * TURN, (k + 1) * TURN)
                nc.vector.tensor_tensor(yT_lo[:, cols], ps_s[k % 2][:, 0:TURN], yT_hi[:, cols].bitcast(fp32),
                                        ALU.subtract).then_inc(y_lo_done, 1)

            for k in range(TURNS):
                dve.wait_ge(turned, k + 2)
                nc.vector.tensor_copy(nodesT[:, k % 2, :], ps_t[(1 + k) % 2][:, :]).then_inc(turn_freed, 1)
                b = k * PER_TURN
                dve.wait_ge(v_hi_done, k + 1)
                nc.vector.tensor_tensor(v[:, b:b + PER_TURN, 1, :], nodes_raw[:, b:b + PER_TURN, :],
                                        v[:, b:b + PER_TURN, 0, :].bitcast(fp32), ALU.subtract)\
                    .then_inc(v_lo_done, 1)
                if k >= 1:
                    y_lo(k - 1)
            y_lo(TURNS - 1)
            for u in range(2):
                relu_h(u, u)
            for u in range(2):
                lo_h(u, u)
            for j in range(SCORES):
                mask(0, 0, j)
            find_max(0, 0)

            def step(t, half, par, at):
                if has(at, 1):
                    mask(t + 1, 1 - par, 0)
                for k in range(TURNS):
                    dve.wait_ge(pT_hi_done, t * TURNS + (k + 1))
                    nc.vector.tensor_tensor(pT_lo[:, k % 2, :], ps_t[turn_bank(k)][:, :],
                                            pT_hi[:, k % 2, :].bitcast(fp32), ALU.subtract)\
                        .then_inc(turn_freed, 1)
                    if k in S_AT and has(at, 1):
                        mask(t + 1, 1 - par, S_AT[k])
                        if S_AT[k] == SCORES - 1:
                            find_max(t + 1, 1 - par)
                    if k == 1 and at != 0:
                        finish(t - 1, half - (1 - par), 1 - par, at is None or at > 2)
                    if k == 1 and has(at, 2):
                        x_stats(t + 2, half + 1, par)
                    if k == H_AT and has(at, 2):
                        relu_h(t + 2, par)
                    if k == H_AT + 2 and has(at, 2):
                        lo_h(t + 2, par)

            steps(dve, step)
            finish(TILES - 1, (TILES - 1) // 2, (TILES - 1) % 2, True)

        @block.tensor
        def _(pe):
            def turn_h(u, s):
                pe.wait_ge(h_done, u + 1)
                nc.tensor.transpose(ps_o[1 - s][:, 0:P], h[:, s, :], ident[:, :]).then_inc(h_turned, 1)

            def scores(u, s, j):
                bank = ps_s[j % 2]
                for part, ys in ((hT_hi, (yT_hi, yT_lo)), (hT_lo, (yT_hi,))):
                    for q in range(SCORE // 512):
                        cols = slice(j * SCORE + q * 512, j * SCORE + (q + 1) * 512)
                        for n, y in enumerate(ys):
                            last = nc.tensor.matmul(bank[:, q * 512:(q + 1) * 512], part[:, s, :], y[:, cols],
                                                    start=(part is hT_hi and n == 0), stop=(part is hT_lo))
                last.then_inc(scores_made, 1)

            def turn(t, s, k):
                for b in range(PER_TURN):
                    col = k * TURN + b * P
                    last = nc.tensor.transpose(ps_t[turn_bank(k)][:, b * P:(b + 1) * P], probs[:, s, col:col + P],
                                               ident[:, :])
                last.then_inc(turned, 1)

            def product(s, k):
                for b in range(PER_TURN):
                    blk = k * PER_TURN + b
                    end = blk == BLOCKS - 1
                    nc.tensor.matmul(ps_o[s][:, 0:2 * D], pT_hi[:, k % 2, b * P:(b + 1) * P],
                                     v[:, blk, :, :].rearrange("p s d -> p (s d)"),
                                     start=(blk == 0), stop=end, skip_group_check=True)
                    last = nc.tensor.matmul(ps_o[s][:, 0:D], pT_lo[:, k % 2, b * P:(b + 1) * P], v[:, blk, 0, :],
                                            start=False, stop=end, skip_group_check=True)
                last.then_inc(pv_done, 1)

            pe.wait_ge(ident_done, 1)
            pe.wait_ge(w_in, 16)
            nc.tensor.transpose(ps_t[0][:, 0:D], w[:, :], ident[:, :]).then_inc(turned, 1)
            pe.wait_ge(nodes_in, 16)

            def y_chunk(k):
                pe.wait_ge(turn_freed, k + 2)
                if k >= 2:
                    pe.wait_ge(y_lo_done, k - 1)
                nc.tensor.matmul(ps_s[k % 2][:, 0:TURN], wT[:, :], nodesT[:, k % 2, :], start=True, stop=True)\
                    .then_inc(y_made, 1)

            for k in range(TURNS):
                if k >= 1:
                    pe.wait_ge(turn_freed, k)
                for b in range(PER_TURN):
                    last = nc.tensor.transpose(ps_t[(1 + k) % 2][:, b * P:(b + 1) * P],
                                               nodes_raw[:, k * PER_TURN + b, :], ident[:, :])
                last.then_inc(turned, 1)
                if k >= 1:
                    y_chunk(k - 1)
            y_chunk(TURNS - 1)
            for u in range(2):
                turn_h(u, u)
            pe.wait_ge(hT_lo_done, 1)
            pe.wait_ge(y_lo_done, TURNS)
            pe.wait_ge(v_lo_done, TURNS)
            for j in range(SCORES):
                if j >= 2:
                    pe.wait_ge(masked, j - 1)
                scores(0, 0, j)

            def step(t, half, par, at):
                more = has(at, 1)

                def next_scores(j):
                    pe.wait_ge(masked, t * SCORES + (SCORES + j - 1))
                    if j == 0:
                        pe.wait_ge(hT_lo_done, t + 2)
                    scores(t + 1, 1 - par, j)

                def next_turn(k):
                    if k % PER_EXP == 0:
                        pe.wait_ge(exp_done, t * SCORES + (k // PER_EXP + 1))
                    pe.wait_ge(turn_freed, turn_no(t, k) - 1)
                    turn(t, par, k)

                if more:
                    next_scores(0)
                next_turn(0)
                for k in range(TURNS):
                    if k + 1 < TURNS:
                        next_turn(k + 1)
                    if k in S_AT and more:
                        next_scores(S_AT[k])
                    if k == 0:
                        pe.wait_ge(hT_done, t + 2 if more else TILES)
                        if at is None or at > 1:
                            pe.wait_ge(fin_done, t - 1)
                    pe.wait_ge(turn_freed, turn_no(t, k) + 1)
                    product(par, k)
                    if k == H_AT and has(at, 2):
                        if at != 0:
                            pe.wait_ge(fin_done, t)
                        turn_h(t + 2, par)

            steps(pe, step)


_INS = ["x", "adj", "L0_gnn_input", "L0_gnn_weight"]


def kernel(**inputs):
    import numpy as _np
    import concourse.bacc as _bacc
    from concourse import mybir as _mybir
    from concourse.bass_utils import run_bass_kernel_spmd as _run

    nc = _bacc.Bacc("TRN2", target_bir_lowering=False, num_devices=1)
    arrays, args = {}, []
    for name in _INS:
        a = _np.ascontiguousarray(inputs[name])
        arrays[f"in_{name}_dram"] = a
        args.append(nc.dram_tensor(f"in_{name}_dram", a.shape, _mybir.dt.from_np(a.dtype), kind="ExternalInput").ap())
    shape = inputs["x"].shape
    args.append(nc.dram_tensor("out_0_dram", shape, _mybir.dt.float32, kind="ExternalOutput").ap())
    gnn_masked_attention_kernel(nc, *args)
    r = _run(nc, [arrays], core_ids=[0])
    return r.results[0]["out_0_dram"]
```

```python
import concourse.bass as bass
from concourse import mybir
from contextlib import ExitStack


def gnn_masked_attention_kernel(
    nc: bass.Bass,
    x: bass.AP,
    adj: bass.AP,
    nodes: bass.AP,
    weight: bass.AP,
    out: bass.AP,
):
    fp32 = mybir.dt.float32
    fp32r = mybir.dt.float32r
    bf16 = mybir.dt.bfloat16
    int32 = mybir.dt.int32
    ALU = mybir.AluOpType
    ACT = mybir.ActivationFunctionType
    AX = mybir.AxisListType

    M, D = x.shape
    N = nodes.shape[0]
    P = 128
    TILES = M // P
    BLOCKS = N // P
    TURN = 512
    TURNS = N // TURN
    PER_TURN = TURN // P
    SCORE = 1024
    SCORES = N // SCORE
    CONV = 2048
    CONVS = N // CONV
    PER_CONV = CONV // SCORE
    PER_EXP = SCORE // TURN
    EPS = 1e-5
    SMALL = 2.0 ** -64
    EXP_SCALE = 2.0 ** 64 / 0.07
    LOWEST = -3.0e38
    AHEAD = 2
    BANKS = 3
    S_AT = {0: 1, 2: 2, 3: 3, 5: 4, 6: 5}
    H_AT = 4
    E_AT = {9: 0, 11: 1}
    E_LATE = {1: 2, 3: 3, 5: 4, 7: 5}

    adj_v = adj.rearrange("(t p) n -> t p n", p=P)
    x_v = x.rearrange("(t p) d -> t p d", p=P)
    out_v = out.rearrange("(t p) d -> t p d", p=P)
    nodes_v = nodes.rearrange("(b p) d -> p b d", p=P)

    ctx = ExitStack()
    with ctx:
        def sb(name, shape, dt):
            return ctx.enter_context(nc.sbuf_tensor(name, shape, dt))

        def pb(name, shape, dt):
            return ctx.enter_context(nc.psum_tensor(name, shape, dt))

        def sem(name):
            return ctx.enter_context(nc.semaphore(name))

        yT_hi = sb("yT_hi", [P, N], fp32r)
        yT_lo = sb("yT_lo", [P, N], fp32r)
        v = sb("v", [P, BLOCKS, 2, D], fp32r)
        probs = sb("probs", [P, 2, N], fp32)
        adj_i = sb("adj_i", [P, CONVS, CONV], int32)
        absent = sb("absent", [P, CONVS, CONV], bf16)
        pT_hi = sb("pT_hi", [P, BANKS, TURN], fp32r)
        pT_lo = sb("pT_lo", [P, BANKS, TURN], fp32r)
        hT = sb("hT", [P, 2, P], fp32)
        hT_hi = sb("hT_hi", [P, 2, P], fp32r)
        hT_lo = sb("hT_lo", [P, 2, P], fp32r)
        h = sb("h", [P, 2, D], fp32)
        x_ln = sb("x_ln", [P, 2, D], fp32)
        x_res = sb("x_res", [P, 2, D], fp32)
        fin_a = sb("fin_a", [P, 2, D], fp32)
        fin = sb("fin", [P, 2, D], fp32)
        ident = sb("ident", [P, P], fp32)
        w = sb("w", [P, D], fp32)
        wT = sb("wT", [P, D], fp32)
        minus_half = sb("minus_half", [P, 1], fp32)
        stats = sb("stats", [P, 2, 6], fp32)
        mean_var = sb("mean_var", [P, 2, 2], fp32)
        var_eps = sb("var_eps", [P, 2, 1], fp32)
        rstd = sb("rstd", [P, 2, 1], fp32)
        chunk_max = sb("chunk_max", [P, 2, SCORES], fp32)
        row_max = sb("row_max", [P, 2, 1], fp32)
        neg_max = sb("neg_max", [P, 2, 1], fp32)
        chunk_sum = sb("chunk_sum", [P, 2, SCORES], fp32)
        row_sum = sb("row_sum", [P, 2, 1], fp32)
        inv_sum = sb("inv_sum", [P, 2, 1], fp32)
        nodes_raw = probs[:, 0, :].rearrange("p (b d) -> p b d", d=D)
        nodesT = probs[:, 1, 0:2 * TURN].rearrange("p (s n) -> p s n", s=2)

        ps_s = [pb(f"ps_s{i}", [P, SCORE], fp32) for i in range(2)]
        ps_t = [pb(f"ps_t{i}", [P, TURN], fp32) for i in range(BANKS)]
        ps_o = pb("ps_o", [P, 2 * D], fp32)

        w_in = sem("w_in")
        nodes_in = sem("nodes_in")
        x_ln_in = [sem(f"x_ln_in{i}") for i in range(2)]
        x_res_in = [sem(f"x_res_in{i}") for i in range(2)]
        adj_in = [sem(f"adj_in{i}") for i in range(CONVS)]
        stored = [sem(f"stored{i}") for i in range(2)]
        ident_zero = sem("ident_zero")
        ident_done = sem("ident_done")
        half_done = sem("half_done")
        absent_done = sem("absent_done")
        stats_done = sem("stats_done")
        aggr_done = sem("aggr_done")
        var_done = sem("var_done")
        rstd_done = sem("rstd_done")
        h_done = sem("h_done")
        h_turned = sem("h_turned")
        hT_hi_done = sem("hT_hi_done")
        hT_lo_done = sem("hT_lo_done")
        turned = sem("turned")
        turn_freed = sem("turn_freed")
        y_made = sem("y_made")
        y_hi_done = sem("y_hi_done")
        y_lo_done = sem("y_lo_done")
        v_hi_done = sem("v_hi_done")
        v_lo_done = sem("v_lo_done")
        scores_made = sem("scores_made")
        taken = sem("taken")
        max_done = sem("max_done")
        neg_max_done = sem("neg_max_done")
        exp_done = sem("exp_done")
        pT_hi_done = sem("pT_hi_done")
        pv_done = sem("pv_done")
        sum_done = sem("sum_done")
        inv_done = sem("inv_done")
        fin_a_done = sem("fin_a_done")
        fin_done = sem("fin_done")

        pool_waited = sem("pool_waited")
        dve_waited = sem("dve_waited")

        SETUP_TURNS = 1 + TURNS

        def turn_no(t, k):
            return t * TURNS + (SETUP_TURNS + k)

        def turn_bank(k):
            return (SETUP_TURNS + k) % BANKS

        H_PLACE = 1 + sum(k < H_AT for k in S_AT)
        ROUND = SCORES + 1

        def score_no(u, j):
            return u * ROUND + (2 + SCORES - ROUND + j + (j >= H_PLACE))

        def h_no(u):
            return u * ROUND + (2 + SCORES - 2 * ROUND + H_PLACE)

        def score_area(u_par, j):
            return ps_s[(u_par * ROUND + 2 + SCORES - ROUND + j + (j >= H_PLACE)) % 2]

        def h_area(u_par):
            return ps_s[(u_par * ROUND + 2 + SCORES + H_PLACE) % 2]

        def steps(eng, step):
            for t in range(3):
                step(t, t % 2, t)
            with eng.Fori(3, TILES - 4, 2) as i:
                step(i, 1, None)
                step(i + 1, 0, None)
            for t in range(TILES - 3, TILES):
                step(t, t % 2, t)

        def loads(u, s):
            return u * 8 + (16 - 8 * s)

        def has(at, ahead):
            return at is None or at + ahead < TILES

        block = ctx.enter_context(nc.Block())

        @block.sync
        def _(sp):
            sp.dma_start(w[:, :], weight).then_inc(w_in, 16)
            sp.dma_start(nodes_raw, nodes_v).then_inc(nodes_in, 16)
            for t in range(2):
                sp.dma_start(x_ln[:, t, :], x_v[t]).then_inc(x_ln_in[t], 16)
            for c in range(CONVS):
                sp.dma_start(adj_i[:, c, :], adj_v[0][:, c * CONV:(c + 1) * CONV]).then_inc(adj_in[c], 16)
            sp.dma_start(x_res[:, 0, :], x_v[0]).then_inc(x_res_in[0], 16)
            sp.wait_ge(h_done, 1)
            sp.dma_start(x_ln[:, 0, :], x_v[2]).then_inc(x_ln_in[0], 16)
            for c in range(CONVS):
                sp.wait_ge(absent_done, c + 1)
                sp.dma_start(adj_i[:, c, :], adj_v[1][:, c * CONV:(c + 1) * CONV]).then_inc(adj_in[c], 16)

            def step(t, par, at):
                if has(at, 3):
                    sp.wait_ge(h_done, t + 2)
                    s = (par + 3) % 2
                    sp.dma_start(x_ln[:, s, :], x_v[t + 3]).then_inc(x_ln_in[s], 16)
                if has(at, 2):
                    for c in range(CONVS):
                        sp.wait_ge(absent_done, t * CONVS + (CONVS + c + 1))
                        sp.dma_start(adj_i[:, c, :], adj_v[t + 2][:, c * CONV:(c + 1) * CONV])\
                            .then_inc(adj_in[c], 16)
                if has(at, 1):
                    if at != 0:
                        sp.wait_ge(fin_done, t)
                    s = (par + 1) % 2
                    sp.dma_start(x_res[:, s, :], x_v[t + 1]).then_inc(x_res_in[s], 16)

            steps(sp, step)

        @block.gpsimd
        def _(pool):
            nc.gpsimd.memset(ident[:, :], 0.0).then_inc(ident_zero, 1)
            nc.gpsimd.memset(minus_half[:, :], -0.5).then_inc(half_done, 1)
            pool.wait_ge(ident_zero, 1)
            nc.gpsimd.affine_select(out=ident[:, :], in_=ident[:, :], compare_op=ALU.not_equal, fill=1.0,
                                    base=0, pattern=[[-1, P]], channel_multiplier=1).then_inc(ident_done, 1)
            pool.wait_ge(half_done, 1)

            def make_h(u, s, free):
                pool.wait_ge(aggr_done, u + 1)
                pool.sem_inc(pool_waited, 1)
                nc.gpsimd.tensor_scalar(var_eps[:, s, :], mean_var[:, s, 1:2], EPS, None, ALU.add)\
                    .then_inc(var_done, 1)
                pool.wait_ge(var_done, u + 1)
                nc.gpsimd.tensor_tensor(rstd[:, s, :], var_eps[:, s, :], minus_half[:, :], ALU.pow)\
                    .then_inc(rstd_done, 1)
                pool.wait_ge(rstd_done, u + 1)
                if free:
                    pool.wait_ge(h_turned, u - 1)
                pool.sem_inc(pool_waited, 1)
                nc.gpsimd.tensor_scalar(h[:, s, :], x_ln[:, s, :], mean_var[:, s, 0:1], rstd[:, s, :],
                                        ALU.subtract, ALU.mult).then_inc(h_done, 1)

            def convert(u, c, free, at=None):
                pool.wait_ge(adj_in[c], u * 16 + 16)
                if free:
                    last = PER_CONV * (c + 1) - 1
                    pool.wait_ge(taken, 2 + last + 1 if at == 0 else score_no(u - 1, last) + 1)
                pool.sem_inc(pool_waited, 1)
                nc.gpsimd.tensor_scalar(absent[:, c, :], adj_i[:, c, :], 0.0, None, ALU.is_le)\
                    .then_inc(absent_done, 1)

            make_h(0, 0, False)
            make_h(1, 1, False)
            for c in range(CONVS):
                convert(0, c, False)

            def step(t, par, at):
                if has(at, 1):
                    for c in range(CONVS):
                        convert(t + 1, c, True, at)
                if has(at, 2):
                    make_h(t + 2, par, True)

            steps(pool, step)

        @block.scalar
        def _(act):
            act.wait_ge(nodes_in, 16)
            for k in range(TURNS):
                b = k * PER_TURN
                nc.scalar.activation(v[:, b:b + PER_TURN, 0, :], nodes_raw[:, b:b + PER_TURN, :], ACT.Copy)\
                    .then_inc(v_hi_done, 1)
                act.wait_ge(y_made, k + 1)
                nc.scalar.activation(yT_hi[:, k * TURN:(k + 1) * TURN], ps_s[k % 2][:, 0:TURN], ACT.Copy)\
                    .then_inc(y_hi_done, 1)

            def split_h(u, s, free):
                act.wait_ge(taken, h_no(u) + 1 if free else u + 1)
                if free:
                    act.wait_ge(scores_made, u * SCORES - SCORES)
                nc.scalar.activation(hT_hi[:, s, :], hT[:, s, :], ACT.Copy).then_inc(hT_hi_done, 1)

            def exp(u, s, c):
                act.wait_ge(neg_max_done, u + 1)
                part = probs[:, s, c * SCORE:(c + 1) * SCORE]
                nc.scalar.activation(part, part, ACT.Exp, bias=neg_max[:, s, :], scale=EXP_SCALE,
                                     accum_out=chunk_sum[:, s, c:c + 1]).then_inc(exp_done, 1)

            split_h(0, 0, False)
            split_h(1, 1, False)
            for c in E_AT.values():
                exp(0, 0, c)

            def step(t, par, at):
                for k in range(TURNS):
                    act.wait_ge(turned, turn_no(t, k) + 1)
                    if k >= BANKS or at != 0:
                        act.wait_ge(pv_done, t * TURNS + (k + 1 - BANKS))
                    nc.scalar.activation(pT_hi[:, k % BANKS, :], ps_t[turn_bank(k)][:, :], ACT.Copy)\
                        .then_inc(pT_hi_done, 1)
                    if k in E_LATE:
                        exp(t, par, E_LATE[k])
                    if k == H_AT + 1 and has(at, 2):
                        split_h(t + 2, par, True)
                    if k == H_AT + 2 and at != 0:
                        act.wait_ge(fin_done, t)
                        act.dma_start(out_v[t - 1], fin[:, 1 - par, :]).then_inc(stored[1 - par], 16)
                    if k in E_AT and has(at, 1):
                        exp(t + 1, 1 - par, E_AT[k])

            steps(act, step)
            act.wait_ge(fin_done, TILES)
            last = (TILES - 1) % 2
            act.dma_start(out_v[TILES - 1], fin[:, last, :]).then_inc(stored[last], 16)
            for s in range(2):
                act.wait_ge(stored[s], 16 * (TILES // 2))

        @block.vector
        def _(dve):
            def x_stats(u, s):
                dve.wait_ge(x_ln_in[s], loads(u, s))
                nc.vector.bn_stats(stats[:, s, :], x_ln[:, s, :]).then_inc(stats_done, 1)
                dve.wait_ge(stats_done, u + 1)
                dve.sem_inc(dve_waited, 1)
                nc.vector.bn_aggr(mean_var[:, s, :], stats[:, s, :]).then_inc(aggr_done, 1)

            def relu_h(u, s, area):
                dve.wait_ge(h_turned, u + 1)
                nc.vector.tensor_scalar(hT[:, s, :], area[:, 0:P], 0.0, SMALL, ALU.max, ALU.mult)\
                    .then_inc(taken, 1)

            def lo_h(u, s):
                dve.wait_ge(hT_hi_done, u + 1)
                nc.vector.tensor_tensor(hT_lo[:, s, :], hT[:, s, :], hT_hi[:, s, :].bitcast(fp32), ALU.subtract)\
                    .then_inc(hT_lo_done, 1)

            def mask(u, s, j, area):
                dve.wait_ge(absent_done, u * CONVS + (j // PER_CONV + 1))
                dve.wait_ge(scores_made, u * SCORES + (j + 1))
                dve.sem_inc(dve_waited, 1)
                c, part = j // PER_CONV, j % PER_CONV
                nc.vector.tensor_tensor_reduce(
                    out=probs[:, s, j * SCORE:(j + 1) * SCORE],
                    in0=area[:, :], in1=absent[:, c, part * SCORE:(part + 1) * SCORE],
                    scale=1.0, scalar=LOWEST, op0=ALU.subtract, op1=ALU.max,
                    accum_out=chunk_max[:, s, j:j + 1]).then_inc(taken, 1)

            def find_max(u, s, chunks):
                dve.wait_ge(taken, chunks)
                nc.vector.tensor_reduce(row_max[:, s, :], chunk_max[:, s, :], AX.X, ALU.max).then_inc(max_done, 1)
                dve.wait_ge(max_done, u + 1)
                nc.vector.tensor_scalar(neg_max[:, s, :], row_max[:, s, :], -EXP_SCALE, None, ALU.mult)\
                    .then_inc(neg_max_done, 1)

            def invert_sum(u, s):
                dve.wait_ge(exp_done, u * SCORES + SCORES)
                nc.vector.reduce_sum(row_sum[:, s, :], chunk_sum[:, s, :], AX.X).then_inc(sum_done, 1)
                dve.wait_ge(sum_done, u + 1)
                nc.vector.reciprocal(inv_sum[:, s, :], row_sum[:, s, :]).then_inc(inv_done, 1)

            def finish(u, s, free):
                dve.wait_ge(inv_done, u + 1)
                dve.wait_ge(x_res_in[s], loads(u, s))
                dve.wait_ge(pv_done, u * TURNS + TURNS)
                nc.vector.scalar_tensor_tensor(out=fin_a[:, s, :], in0=ps_o[:, 0:D], scalar=inv_sum[:, s, :],
                                               in1=x_res[:, s, :], op0=ALU.mult, op1=ALU.add)\
                    .then_inc(fin_a_done, 1)
                dve.wait_ge(fin_a_done, u + 1)
                if free:
                    dve.wait_ge(stored[s], loads(u - 2, s))
                nc.vector.scalar_tensor_tensor(out=fin[:, s, :], in0=ps_o[:, D:2 * D], scalar=inv_sum[:, s, :],
                                               in1=fin_a[:, s, :], op0=ALU.mult, op1=ALU.add)\
                    .then_inc(fin_done, 1)

            dve.wait_ge(turned, 1)
            nc.vector.tensor_copy(wT[:, :], ps_t[0][:, 0:D]).then_inc(turn_freed, 1)
            x_stats(0, 0)
            x_stats(1, 1)

            def y_lo(k):
                dve.wait_ge(y_hi_done, k + 1)
                cols = slice(k * TURN, (k + 1) * TURN)
                nc.vector.tensor_tensor(yT_lo[:, cols], ps_s[k % 2][:, 0:TURN], yT_hi[:, cols].bitcast(fp32),
                                        ALU.subtract).then_inc(y_lo_done, 1)

            for k in range(TURNS):
                dve.wait_ge(turned, k + 2)
                nc.vector.tensor_copy(nodesT[:, k % 2, :], ps_t[(1 + k) % BANKS][:, :]).then_inc(turn_freed, 1)
                b = k * PER_TURN
                dve.wait_ge(v_hi_done, k + 1)
                nc.vector.tensor_tensor(v[:, b:b + PER_TURN, 1, :], nodes_raw[:, b:b + PER_TURN, :],
                                        v[:, b:b + PER_TURN, 0, :].bitcast(fp32), ALU.subtract)\
                    .then_inc(v_lo_done, 1)
                if k >= 1:
                    y_lo(k - 1)
            y_lo(TURNS - 1)
            for u in range(2):
                relu_h(u, u, ps_s[u])
            for u in range(2):
                lo_h(u, u)
            for j in range(SCORES):
                mask(0, 0, j, ps_s[j % 2])
            find_max(0, 0, 2 + SCORES)

            def step(t, par, at):
                nxt = 1 - par
                if at != 0:
                    finish(t - 1, nxt, at is None or at > 2)
                if has(at, 1):
                    mask(t + 1, nxt, 0, score_area(nxt, 0))
                for k in range(TURNS):
                    dve.wait_ge(pT_hi_done, t * TURNS + (k + 1))
                    nc.vector.tensor_tensor(pT_lo[:, k % BANKS, :], ps_t[turn_bank(k)][:, :],
                                            pT_hi[:, k % BANKS, :].bitcast(fp32), ALU.subtract)\
                        .then_inc(turn_freed, 1)
                    if k - 1 in S_AT and has(at, 1):
                        j = S_AT[k - 1]
                        mask(t + 1, nxt, j, score_area(nxt, j))
                        if j == SCORES - 1:
                            find_max(t + 1, nxt, score_no(t + 1, j) + 1)
                    if k == 1 and has(at, 2):
                        x_stats(t + 2, par)
                    if k == H_AT + 1:
                        if has(at, 2):
                            relu_h(t + 2, par, h_area(par))
                        elif has(at, 1):
                            nc.vector.memset(hT[:, par, 0:1], 0.0).then_inc(taken, 1)
                    if k == H_AT + 3 and has(at, 2):
                        lo_h(t + 2, par)
                    if k == TURNS - 2:
                        invert_sum(t, par)

            steps(dve, step)
            finish(TILES - 1, (TILES - 1) % 2, True)

        @block.tensor
        def _(pe):
            def turn_h(u, s, area):
                pe.wait_ge(h_done, u + 1)
                nc.tensor.transpose(area[:, 0:P], h[:, s, :], ident[:, :]).then_inc(h_turned, 1)

            def scores(s, j, area):
                for part, ys in ((hT_hi, (yT_hi, yT_lo)), (hT_lo, (yT_hi,))):
                    for q in range(SCORE // 512):
                        cols = slice(j * SCORE + q * 512, j * SCORE + (q + 1) * 512)
                        for n, y in enumerate(ys):
                            last = nc.tensor.matmul(area[:, q * 512:(q + 1) * 512], part[:, s, :], y[:, cols],
                                                    start=(part is hT_hi and n == 0), stop=(part is hT_lo))
                last.then_inc(scores_made, 1)

            def turn(t, s, k):
                for b in range(PER_TURN):
                    col = k * TURN + b * P
                    last = nc.tensor.transpose(ps_t[turn_bank(k)][:, b * P:(b + 1) * P], probs[:, s, col:col + P],
                                               ident[:, :])
                last.then_inc(turned, 1)

            def product(k):
                for b in range(PER_TURN):
                    blk = k * PER_TURN + b
                    end = blk == BLOCKS - 1
                    nc.tensor.matmul(ps_o[:, 0:2 * D], pT_hi[:, k % BANKS, b * P:(b + 1) * P],
                                     v[:, blk, :, :].rearrange("p s d -> p (s d)"),
                                     start=(blk == 0), stop=end, skip_group_check=True)
                    last = nc.tensor.matmul(ps_o[:, 0:D], pT_lo[:, k % BANKS, b * P:(b + 1) * P], v[:, blk, 0, :],
                                            start=False, stop=end, skip_group_check=True)
                last.then_inc(pv_done, 1)

            pe.wait_ge(ident_done, 1)
            pe.wait_ge(w_in, 16)
            nc.tensor.transpose(ps_t[0][:, 0:D], w[:, :], ident[:, :]).then_inc(turned, 1)
            pe.wait_ge(nodes_in, 16)

            def y_chunk(k):
                pe.wait_ge(turn_freed, k + 2)
                if k >= 2:
                    pe.wait_ge(y_lo_done, k - 1)
                nc.tensor.matmul(ps_s[k % 2][:, 0:TURN], wT[:, :], nodesT[:, k % 2, :], start=True, stop=True)\
                    .then_inc(y_made, 1)

            for k in range(TURNS):
                if k + 1 >= BANKS:
                    pe.wait_ge(turn_freed, k + 2 - BANKS)
                for b in range(PER_TURN):
                    last = nc.tensor.transpose(ps_t[(1 + k) % BANKS][:, b * P:(b + 1) * P],
                                               nodes_raw[:, k * PER_TURN + b, :], ident[:, :])
                last.then_inc(turned, 1)
                if k >= 1:
                    y_chunk(k - 1)
            y_chunk(TURNS - 1)
            pe.wait_ge(y_lo_done, TURNS)
            pe.wait_ge(v_lo_done, TURNS)
            for u in range(2):
                turn_h(u, u, ps_s[u])
            pe.wait_ge(hT_lo_done, 1)
            for j in range(SCORES):
                pe.wait_ge(taken, j + 1)
                scores(0, j, ps_s[j % 2])

            def step(t, par, at):
                nxt = 1 - par

                def next_scores(j):
                    pe.wait_ge(taken, score_no(t + 1, j) - 1)
                    if j == 0:
                        pe.wait_ge(hT_lo_done, t + 2)
                    scores(nxt, j, score_area(nxt, j))

                def next_turn(k):
                    if k % PER_EXP == 0:
                        pe.wait_ge(exp_done, t * SCORES + (k // PER_EXP + 1))
                    pe.wait_ge(turn_freed, turn_no(t, k) + 1 - BANKS)
                    turn(t, par, k)

                if has(at, 1):
                    next_scores(0)
                for k in range(AHEAD):
                    next_turn(k)
                for k in range(TURNS):
                    if k + AHEAD < TURNS:
                        next_turn(k + AHEAD)
                    if k in S_AT and has(at, 1):
                        next_scores(S_AT[k])
                    if k == H_AT and has(at, 2):
                        pe.wait_ge(taken, h_no(t + 2) - 1)
                        turn_h(t + 2, par, h_area(par))
                    if k == 0 and at != 0:
                        pe.wait_ge(fin_done, t)
                    pe.wait_ge(turn_freed, turn_no(t, k) + 1)
                    product(k)

            steps(pe, step)


_INS = ["x", "adj", "L0_gnn_input", "L0_gnn_weight"]


def kernel(**inputs):
    import numpy as _np
    import concourse.bacc as _bacc
    from concourse import mybir as _mybir
    from concourse.bass_utils import run_bass_kernel_spmd as _run

    nc = _bacc.Bacc("TRN2", target_bir_lowering=False, num_devices=1)
    arrays, args = {}, []
    for name in _INS:
        a = _np.ascontiguousarray(inputs[name])
        arrays[f"in_{name}_dram"] = a
        args.append(nc.dram_tensor(f"in_{name}_dram", a.shape, _mybir.dt.from_np(a.dtype), kind="ExternalInput").ap())
    shape = inputs["x"].shape
    args.append(nc.dram_tensor("out_0_dram", shape, _mybir.dt.float32, kind="ExternalOutput").ap())
    gnn_masked_attention_kernel(nc, *args)
    r = _run(nc, [arrays], core_ids=[0])
    return r.results[0]["out_0_dram"]
```

```python
import concourse.bass as bass
from concourse import mybir
from contextlib import ExitStack


def gnn_masked_attention_kernel(
    nc: bass.Bass,
    x: bass.AP,
    adj: bass.AP,
    nodes: bass.AP,
    weight: bass.AP,
    out: bass.AP,
):
    fp32 = mybir.dt.float32
    fp32r = mybir.dt.float32r
    bf16 = mybir.dt.bfloat16
    fp16 = mybir.dt.float16
    int32 = mybir.dt.int32
    ALU = mybir.AluOpType
    ACT = mybir.ActivationFunctionType
    AX = mybir.AxisListType

    M, D = x.shape
    N = nodes.shape[0]
    P = 128
    TILES = M // P
    BLOCKS = N // P
    TURN = 512
    TURNS = N // TURN
    PER_TURN = TURN // P
    SCORE = 1024
    SCORES = N // SCORE
    CONV = 2048
    CONVS = N // CONV
    PER_CONV = CONV // SCORE
    PER_EXP = SCORE // TURN
    PARTS = 4
    PART = BLOCKS // PARTS
    PART_TURNS = TURNS // PARTS
    EXPONENT = 0xFF << 23
    NODES_TOP = 14
    LEAST_FIELD = 16
    EPS = 1e-5
    SMALL = 2.0 ** -64
    EXP_SCALE = 2.0 ** 64 / 0.07
    LOWEST = -3.0e38
    AHEAD = 2
    BANKS = 3
    S_AT = {0: 1, 2: 2, 3: 3, 5: 4, 6: 5}
    H_AT = 4
    E_EARLY = (0, 1)
    E_LATE = {1: 2, 3: 3, 5: 4, 7: 5}

    adj_v = adj.rearrange("(t p) n -> t p n", p=P)
    x_v = x.rearrange("(t p) d -> t p d", p=P)
    out_v = out.rearrange("(t p) d -> t p d", p=P)
    nodes_v = nodes.rearrange("(b p) d -> p b d", p=P)

    ctx = ExitStack()
    with ctx:
        def sb(name, shape, dt):
            return ctx.enter_context(nc.sbuf_tensor(name, shape, dt))

        def pb(name, shape, dt):
            return ctx.enter_context(nc.psum_tensor(name, shape, dt))

        def sem(name):
            return ctx.enter_context(nc.semaphore(name))

        yT_hi = sb("yT_hi", [P, N], fp32r)
        yT_lo = sb("yT_lo", [P, N], fp32r)
        v = sb("v", [P, BLOCKS, 2, D], fp16)
        nodes_raw = sb("nodes_raw", [P, BLOCKS, D], fp32)
        probs = sb("probs", [P, 2, N], fp32)
        adj_i = sb("adj_i", [P, CONVS, CONV], int32)
        absent = sb("absent", [P, CONVS, CONV], bf16)
        pT_hi = sb("pT_hi", [P, BANKS, TURN], fp16)
        pT_lo = sb("pT_lo", [P, BANKS, TURN], fp16)
        hT = sb("hT", [P, 2, P], fp32)
        hT_hi = sb("hT_hi", [P, 2, P], fp32r)
        hT_lo = sb("hT_lo", [P, 2, P], fp32r)
        h = sb("h", [P, 2, D], fp32)
        x_ln = sb("x_ln", [P, 2, D], fp32)
        x_res = sb("x_res", [P, 2, D], fp32)
        fin_a = sb("fin_a", [P, 2, D], fp32)
        fin = sb("fin", [P, 2, D], fp32)
        ident = sb("ident", [P, P], fp32)
        w = sb("w", [P, D], fp32)
        wT = sb("wT", [P, D], fp32)
        minus_half = sb("minus_half", [P, 1], fp32)
        stats = sb("stats", [P, 2, 6], fp32)
        mean_var = sb("mean_var", [P, 2, 2], fp32)
        var_eps = sb("var_eps", [P, 2, 1], fp32)
        rstd = sb("rstd", [P, 2, 1], fp32)
        chunk_max = sb("chunk_max", [P, 2, SCORES], fp32)
        row_max = sb("row_max", [P, 2, 1], fp32)
        neg_max = sb("neg_max", [P, 2, 1], fp32)
        chunk_sum = sb("chunk_sum", [P, 2, SCORES], fp32)
        row_sum = sb("row_sum", [P, 2, 1], fp32)
        recip = sb("recip", [P, 2, 1], fp32)
        inv_sum = sb("inv_sum", [P, 2, 1], fp32)
        part_max = sb("part_max", [P, PARTS], fp32)
        nodes_max = sb("nodes_max", [P, 1], fp32)
        nodes_top = sb("nodes_top", [P, 1], fp32)
        field = sb("field", [P, 1], int32)
        down = sb("down", [P, 1], int32)
        scale_bits = sb("scale_bits", [P, 1], int32)
        unscale_bits = sb("unscale_bits", [P, 1], int32)
        scale = scale_bits[:, :].bitcast(fp32)
        unscale = unscale_bits[:, :].bitcast(fp32)
        nodesT = probs[:, 1, 0:2 * TURN].rearrange("p (s n) -> p s n", s=2)

        ps_s = [pb(f"ps_s{i}", [P, SCORE], fp32) for i in range(2)]
        ps_t = [pb(f"ps_t{i}", [P, TURN], fp32) for i in range(BANKS)]
        ps_o = pb("ps_o", [P, 512], fp32)

        w_in = sem("w_in")
        nodes_in = [sem(f"nodes_in{i}") for i in range(PARTS)]
        x_ln_in = [sem(f"x_ln_in{i}") for i in range(2)]
        x_res_in = [sem(f"x_res_in{i}") for i in range(2)]
        adj_in = [sem(f"adj_in{i}") for i in range(CONVS)]
        stored = [sem(f"stored{i}") for i in range(2)]
        ident_zero = sem("ident_zero")
        ident_done = sem("ident_done")
        half_done = sem("half_done")
        absent_done = sem("absent_done")
        stats_done = sem("stats_done")
        aggr_done = sem("aggr_done")
        var_done = sem("var_done")
        rstd_done = sem("rstd_done")
        h_done = sem("h_done")
        h_turned = sem("h_turned")
        hT_hi_done = sem("hT_hi_done")
        hT_lo_done = sem("hT_lo_done")
        turned = sem("turned")
        w_turned = sem("w_turned")
        wT_done = sem("wT_done")
        nodes_turned = sem("nodes_turned")
        nodesT_done = sem("nodesT_done")
        part_max_done = sem("part_max_done")
        nodes_max_done = sem("nodes_max_done")
        nodes_top_done = sem("nodes_top_done")
        scale_steps = sem("scale_steps")
        turn_freed = sem("turn_freed")
        y_made = sem("y_made")
        y_hi_done = sem("y_hi_done")
        y_lo_done = sem("y_lo_done")
        v_hi_done = sem("v_hi_done")
        v_lo_done = sem("v_lo_done")
        scores_made = sem("scores_made")
        taken = sem("taken")
        max_done = sem("max_done")
        neg_max_done = sem("neg_max_done")
        exp_done = sem("exp_done")
        pT_hi_done = sem("pT_hi_done")
        pv_done = sem("pv_done")
        sum_done = sem("sum_done")
        recip_done = sem("recip_done")
        inv_done = sem("inv_done")
        fin_a_done = sem("fin_a_done")
        fin_done = sem("fin_done")

        pool_waited = sem("pool_waited")
        dve_waited = sem("dve_waited")

        def turn_no(t, k):
            return t * TURNS + k

        nodes_bank = ps_t[0:2]
        y_bank = [ps_t[2], ps_o]

        H_PLACE = 1 + sum(k < H_AT for k in S_AT)
        ROUND = SCORES + 1

        def score_no(u, j):
            return u * ROUND + (2 + SCORES - ROUND + j + (j >= H_PLACE))

        def h_no(u):
            return u * ROUND + (2 + SCORES - 2 * ROUND + H_PLACE)

        def score_area(u_par, j):
            return ps_s[(u_par * ROUND + 2 + SCORES - ROUND + j + (j >= H_PLACE)) % 2]

        def h_area(u_par):
            return ps_s[(u_par * ROUND + 2 + SCORES + H_PLACE) % 2]

        def steps(eng, step):
            for t in range(3):
                step(t, t % 2, t)
            with eng.Fori(3, TILES - 4, 2) as i:
                step(i, 1, None)
                step(i + 1, 0, None)
            for t in range(TILES - 3, TILES):
                step(t, t % 2, t)

        def loads(u, s):
            return u * 8 + (16 - 8 * s)

        def has(at, ahead):
            return at is None or at + ahead < TILES

        block = ctx.enter_context(nc.Block())

        @block.sync
        def _(sp):
            sp.dma_start(w[:, :], weight).then_inc(w_in, 16)
            for t in range(2):
                sp.dma_start(x_ln[:, t, :], x_v[t]).then_inc(x_ln_in[t], 16)
            for i in range(PARTS):
                blocks = slice(i * PART, (i + 1) * PART)
                sp.dma_start(nodes_raw[:, blocks, :], nodes_v[:, blocks, :]).then_inc(nodes_in[i], 16)
                if i != 1:
                    c = max(i - 1, 0)
                    sp.dma_start(adj_i[:, c, :], adj_v[0][:, c * CONV:(c + 1) * CONV]).then_inc(adj_in[c], 16)
            sp.dma_start(x_res[:, 0, :], x_v[0]).then_inc(x_res_in[0], 16)
            sp.wait_ge(h_done, 1)
            sp.dma_start(x_ln[:, 0, :], x_v[2]).then_inc(x_ln_in[0], 16)
            for c in range(CONVS):
                sp.wait_ge(absent_done, c + 1)
                sp.dma_start(adj_i[:, c, :], adj_v[1][:, c * CONV:(c + 1) * CONV]).then_inc(adj_in[c], 16)

            def step(t, par, at):
                if has(at, 3):
                    sp.wait_ge(h_done, t + 2)
                    s = (par + 3) % 2
                    sp.dma_start(x_ln[:, s, :], x_v[t + 3]).then_inc(x_ln_in[s], 16)
                if has(at, 2):
                    for c in range(CONVS):
                        sp.wait_ge(absent_done, t * CONVS + (CONVS + c + 1))
                        sp.dma_start(adj_i[:, c, :], adj_v[t + 2][:, c * CONV:(c + 1) * CONV])\
                            .then_inc(adj_in[c], 16)
                if has(at, 1):
                    if at != 0:
                        sp.wait_ge(fin_done, t)
                    s = (par + 1) % 2
                    sp.dma_start(x_res[:, s, :], x_v[t + 1]).then_inc(x_res_in[s], 16)

            steps(sp, step)

        @block.gpsimd
        def _(pool):
            nc.gpsimd.memset(ident[:, :], 0.0).then_inc(ident_zero, 1)
            nc.gpsimd.memset(minus_half[:, :], -0.5).then_inc(half_done, 1)
            pool.wait_ge(ident_zero, 1)
            nc.gpsimd.affine_select(out=ident[:, :], in_=ident[:, :], compare_op=ALU.not_equal, fill=1.0,
                                    base=0, pattern=[[-1, P]], channel_multiplier=1).then_inc(ident_done, 1)
            pool.wait_ge(half_done, 1)

            def make_h(u, s, free):
                pool.wait_ge(aggr_done, u + 1)
                pool.sem_inc(pool_waited, 1)
                nc.gpsimd.tensor_scalar(var_eps[:, s, :], mean_var[:, s, 1:2], EPS, None, ALU.add)\
                    .then_inc(var_done, 1)
                pool.wait_ge(var_done, u + 1)
                nc.gpsimd.tensor_tensor(rstd[:, s, :], var_eps[:, s, :], minus_half[:, :], ALU.pow)\
                    .then_inc(rstd_done, 1)
                pool.wait_ge(rstd_done, u + 1)
                if free:
                    pool.wait_ge(h_turned, u - 1)
                pool.sem_inc(pool_waited, 1)
                nc.gpsimd.tensor_scalar(h[:, s, :], x_ln[:, s, :], mean_var[:, s, 0:1], rstd[:, s, :],
                                        ALU.subtract, ALU.mult).then_inc(h_done, 1)

            def convert(u, c, free, at=None):
                pool.wait_ge(adj_in[c], u * 16 + 16)
                if free:
                    last = PER_CONV * (c + 1) - 1
                    pool.wait_ge(taken, 2 + last + 1 if at == 0 else score_no(u - 1, last) + 1)
                pool.sem_inc(pool_waited, 1)
                nc.gpsimd.tensor_scalar(absent[:, c, :], adj_i[:, c, :], 0.0, None, ALU.is_le)\
                    .then_inc(absent_done, 1)

            make_h(0, 0, False)
            make_h(1, 1, False)
            for c in range(CONVS):
                convert(0, c, False)
            pool.wait_ge(nodes_max_done, 1)
            nc.gpsimd.partition_all_reduce(nodes_top[:, :], nodes_max[:, :], P, bass.bass_isa.ReduceOp.max)\
                .then_inc(nodes_top_done, 1)

            def step(t, par, at):
                if has(at, 1):
                    for c in range(CONVS):
                        convert(t + 1, c, True, at)
                if has(at, 2):
                    make_h(t + 2, par, True)

            steps(pool, step)

        @block.scalar
        def _(act):
            def split_h(u, s, free):
                act.wait_ge(taken, h_no(u) + 1 if free else u + 1)
                if free:
                    act.wait_ge(scores_made, u * SCORES - SCORES)
                nc.scalar.activation(hT_hi[:, s, :], hT[:, s, :], ACT.Copy).then_inc(hT_hi_done, 1)

            def exp(u, s, c):
                act.wait_ge(neg_max_done, u + 1)
                part = probs[:, s, c * SCORE:(c + 1) * SCORE]
                nc.scalar.activation(part, part, ACT.Exp, bias=neg_max[:, s, :], scale=EXP_SCALE,
                                     accum_out=chunk_sum[:, s, c:c + 1]).then_inc(exp_done, 1)

            def v_hi(i):
                if i == 0:
                    act.wait_ge(scale_steps, 4)
                blocks = slice(i * PART, (i + 1) * PART)
                nc.scalar.activation(v[:, blocks, 0, :], nodes_raw[:, blocks, :], ACT.Copy, scale=scale)\
                    .then_inc(v_hi_done, 1)

            for k in range(TURNS + 1):
                if k < TURNS:
                    act.wait_ge(nodes_turned, k + 1)
                    if k >= 2:
                        act.wait_ge(y_made, k - 1)
                    nc.scalar.activation(nodesT[:, k % 2, :], nodes_bank[k % 2][:, :], ACT.Copy)\
                        .then_inc(nodesT_done, 1)
                if k >= 1:
                    act.wait_ge(y_made, k)
                    nc.scalar.activation(yT_hi[:, (k - 1) * TURN:k * TURN], y_bank[(k - 1) % 2][:, :], ACT.Copy)\
                        .then_inc(y_hi_done, 1)
                if k == 1:
                    for u in range(2):
                        split_h(u, u, False)
            for i in range(2):
                v_hi(i)
            for c in E_EARLY:
                exp(0, 0, c)

            def step(t, par, at):
                for k in range(TURNS):
                    act.wait_ge(turned, turn_no(t, k) + 1)
                    if k >= BANKS or at != 0:
                        act.wait_ge(pv_done, t * TURNS + (k + 1 - BANKS))
                    nc.scalar.activation(pT_hi[:, k % BANKS, :], ps_t[k % BANKS][:, :], ACT.Copy)\
                        .then_inc(pT_hi_done, 1)
                    if k in E_LATE:
                        exp(t, par, E_LATE[k])
                    if at == 0 and k in (2, 6):
                        v_hi(2 + k // 6)
                    if k == H_AT + 1 and has(at, 2):
                        split_h(t + 2, par, True)
                    if k == H_AT + 2 and at != 0:
                        act.wait_ge(fin_done, t)
                        act.dma_start(out_v[t - 1], fin[:, 1 - par, :]).then_inc(stored[1 - par], 16)
                if has(at, 1):
                    for c in E_EARLY:
                        exp(t + 1, 1 - par, c)

            steps(act, step)
            act.wait_ge(fin_done, TILES)
            last = (TILES - 1) % 2
            act.dma_start(out_v[TILES - 1], fin[:, last, :]).then_inc(stored[last], 16)
            for s in range(2):
                act.wait_ge(stored[s], 16 * (TILES // 2))

        @block.vector
        def _(dve):
            def x_stats(u, s):
                dve.wait_ge(x_ln_in[s], loads(u, s))
                nc.vector.bn_stats(stats[:, s, :], x_ln[:, s, :]).then_inc(stats_done, 1)
                dve.wait_ge(stats_done, u + 1)
                dve.sem_inc(dve_waited, 1)
                nc.vector.bn_aggr(mean_var[:, s, :], stats[:, s, :]).then_inc(aggr_done, 1)

            def relu_h(u, s, area):
                dve.wait_ge(h_turned, u + 1)
                nc.vector.tensor_scalar(hT[:, s, :], area[:, 0:P], 0.0, SMALL, ALU.max, ALU.mult)\
                    .then_inc(taken, 1)

            def lo_h(u, s):
                dve.wait_ge(hT_hi_done, u + 1)
                nc.vector.tensor_tensor(hT_lo[:, s, :], hT[:, s, :], hT_hi[:, s, :].bitcast(fp32), ALU.subtract)\
                    .then_inc(hT_lo_done, 1)

            def mask(u, s, j, area):
                dve.wait_ge(absent_done, u * CONVS + (j // PER_CONV + 1))
                dve.wait_ge(scores_made, u * SCORES + (j + 1))
                dve.sem_inc(dve_waited, 1)
                c, part = j // PER_CONV, j % PER_CONV
                nc.vector.tensor_tensor_reduce(
                    out=probs[:, s, j * SCORE:(j + 1) * SCORE],
                    in0=area[:, :], in1=absent[:, c, part * SCORE:(part + 1) * SCORE],
                    scale=1.0, scalar=LOWEST, op0=ALU.subtract, op1=ALU.max,
                    accum_out=chunk_max[:, s, j:j + 1]).then_inc(taken, 1)

            def find_max(u, s, chunks):
                dve.wait_ge(taken, chunks)
                nc.vector.tensor_reduce(row_max[:, s, :], chunk_max[:, s, :], AX.X, ALU.max).then_inc(max_done, 1)

            def negate_max(u, s):
                dve.wait_ge(max_done, u + 1)
                nc.vector.tensor_scalar(neg_max[:, s, :], row_max[:, s, :], -EXP_SCALE, None, ALU.mult)\
                    .then_inc(neg_max_done, 1)

            def invert_sum(u, s):
                dve.wait_ge(exp_done, u * SCORES + SCORES)
                nc.vector.reduce_sum(row_sum[:, s, :], chunk_sum[:, s, :], AX.X).then_inc(sum_done, 1)
                dve.wait_ge(sum_done, u + 1)
                nc.vector.reciprocal(recip[:, s, :], row_sum[:, s, :]).then_inc(recip_done, 1)
                dve.wait_ge(recip_done, u + 1)
                nc.vector.tensor_scalar(inv_sum[:, s, :], recip[:, s, :], unscale, None, ALU.mult)\
                    .then_inc(inv_done, 1)

            def finish(u, s, free):
                dve.wait_ge(inv_done, u + 1)
                dve.wait_ge(x_res_in[s], loads(u, s))
                dve.wait_ge(pv_done, u * TURNS + TURNS)
                nc.vector.scalar_tensor_tensor(out=fin_a[:, s, :], in0=ps_o[:, 0:D], scalar=inv_sum[:, s, :],
                                               in1=x_res[:, s, :], op0=ALU.mult, op1=ALU.add)\
                    .then_inc(fin_a_done, 1)
                dve.wait_ge(fin_a_done, u + 1)
                if free:
                    dve.wait_ge(stored[s], loads(u - 2, s))
                nc.vector.scalar_tensor_tensor(out=fin[:, s, :], in0=ps_o[:, D:2 * D], scalar=inv_sum[:, s, :],
                                               in1=fin_a[:, s, :], op0=ALU.mult, op1=ALU.add)\
                    .then_inc(fin_done, 1)

            def y_lo(k):
                dve.wait_ge(y_hi_done, k + 1)
                cols = slice(k * TURN, (k + 1) * TURN)
                nc.vector.tensor_tensor(yT_lo[:, cols], y_bank[k % 2][:, :], yT_hi[:, cols].bitcast(fp32),
                                        ALU.subtract).then_inc(y_lo_done, 1)

            def v_lo(i):
                dve.wait_ge(v_hi_done, i + 1)
                dve.wait_ge(scale_steps, 4)
                blocks = slice(i * PART, (i + 1) * PART)
                nc.vector.scalar_tensor_tensor(out=v[:, blocks, 1, :], in0=nodes_raw[:, blocks, :], scalar=scale,
                                               in1=v[:, blocks, 0, :], op0=ALU.mult, op1=ALU.subtract)\
                    .then_inc(v_lo_done, 1)

            def nodes_scale():
                dve.wait_ge(nodes_top_done, 1)
                nc.vector.tensor_scalar(field[:, :], nodes_top[:, :].bitcast(int32), EXPONENT, None,
                                        ALU.bitwise_and).then_inc(scale_steps, 1)
                dve.wait_ge(scale_steps, 1)
                nc.vector.tensor_scalar(down[:, :], field[:, :], float(LEAST_FIELD << 23),
                                        float((2 * 127 + NODES_TOP) << 23), ALU.max, ALU.subtract)\
                    .then_inc(scale_steps, 1)
                nc.vector.tensor_scalar(unscale_bits[:, :], field[:, :], float(LEAST_FIELD << 23),
                                        float(NODES_TOP << 23), ALU.max, ALU.subtract).then_inc(scale_steps, 1)
                dve.wait_ge(scale_steps, 3)
                nc.vector.tensor_scalar(scale_bits[:, :], down[:, :], -1.0, None, ALU.mult)\
                    .then_inc(scale_steps, 1)

            dve.wait_ge(w_turned, 1)
            nc.vector.tensor_copy(wT[:, :], ps_o[:, 0:D]).then_inc(wT_done, 1)
            x_stats(0, 0)
            x_stats(1, 1)

            def find_part_max(i):
                dve.wait_ge(nodes_in[i], 16)
                nc.vector.tensor_reduce(part_max[:, i:i + 1], nodes_raw[:, i * PART:(i + 1) * PART, :], AX.XY,
                                        ALU.max, apply_absolute_value=True).then_inc(part_max_done, 1)

            find_part_max(0)
            for u in range(2):
                relu_h(u, u, ps_s[u])
            for k in range(TURNS):
                y_lo(k)
                if k == 1:
                    for u in range(2):
                        lo_h(u, u)
                if k in (2, 3, 5):
                    find_part_max({2: 1, 3: 2, 5: 3}[k])
                if k == 6:
                    dve.wait_ge(part_max_done, PARTS)
                    nc.vector.reduce_max(nodes_max[:, :], part_max[:, :], AX.X).then_inc(nodes_max_done, 1)
                if k == 8:
                    nodes_scale()
                if k >= 4 and k % 2 == 0:
                    mask(0, 0, k // 2 - 2, ps_s[k // 2 % 2])
            mask(0, 0, SCORES - 2, ps_s[(SCORES - 2) % 2])
            mask(0, 0, SCORES - 1, ps_s[(SCORES - 1) % 2])
            find_max(0, 0, 2 + SCORES)
            negate_max(0, 0)
            v_lo(0)

            def step(t, par, at):
                nxt = 1 - par
                if at != 0:
                    finish(t - 1, nxt, at is None or at > 2)
                if at == 0:
                    mask(1, 1, 0, score_area(1, 0))
                for k in range(TURNS):
                    dve.wait_ge(pT_hi_done, t * TURNS + (k + 1))
                    nc.vector.tensor_tensor(pT_lo[:, k % BANKS, :], ps_t[k % BANKS][:, :],
                                            pT_hi[:, k % BANKS, :], ALU.subtract)\
                        .then_inc(turn_freed, 1)
                    if k >= 2 and S_AT.get(k - 2) == SCORES - 1 and has(at, 1):
                        find_max(t + 1, nxt, score_no(t + 1, SCORES - 1) + 1)
                    if k >= 3 and S_AT.get(k - 3) == SCORES - 1 and has(at, 1):
                        negate_max(t + 1, nxt)
                    if k - 1 in S_AT and has(at, 1):
                        j = S_AT[k - 1]
                        mask(t + 1, nxt, j, score_area(nxt, j))
                    if at == 0 and k in (2, 5, 8):
                        v_lo(1 + k // 3)
                    if k == 1 and has(at, 2):
                        x_stats(t + 2, par)
                    if k == H_AT + 1:
                        if has(at, 2):
                            relu_h(t + 2, par, h_area(par))
                        elif has(at, 1):
                            nc.vector.memset(hT[:, par, 0:1], 0.0).then_inc(taken, 1)
                    if k == H_AT + 5 and has(at, 2):
                        lo_h(t + 2, par)
                    if k == TURNS - 1:
                        invert_sum(t, par)
                if has(at, 2):
                    mask(t + 2, par, 0, score_area(par, 0))

            steps(dve, step)
            finish(TILES - 1, (TILES - 1) % 2, True)

        @block.tensor
        def _(pe):
            def turn_h(u, s, area):
                pe.wait_ge(h_done, u + 1)
                nc.tensor.transpose(area[:, 0:P], h[:, s, :], ident[:, :]).then_inc(h_turned, 1)

            def scores(s, j, area):
                for part, ys in ((hT_hi, (yT_hi, yT_lo)), (hT_lo, (yT_hi,))):
                    for q in range(SCORE // 512):
                        cols = slice(j * SCORE + q * 512, j * SCORE + (q + 1) * 512)
                        for n, y in enumerate(ys):
                            last = nc.tensor.matmul(area[:, q * 512:(q + 1) * 512], part[:, s, :], y[:, cols],
                                                    start=(part is hT_hi and n == 0), stop=(part is hT_lo))
                last.then_inc(scores_made, 1)

            def turn(t, s, k):
                for b in range(PER_TURN):
                    col = k * TURN + b * P
                    last = nc.tensor.transpose(ps_t[k % BANKS][:, b * P:(b + 1) * P], probs[:, s, col:col + P],
                                               ident[:, :])
                last.then_inc(turned, 1)

            def product(k):
                for b in range(PER_TURN):
                    blk = k * PER_TURN + b
                    end = blk == BLOCKS - 1
                    nc.tensor.matmul(ps_o[:, 0:2 * D], pT_hi[:, k % BANKS, b * P:(b + 1) * P],
                                     v[:, blk, :, :].rearrange("p s d -> p (s d)"),
                                     start=(blk == 0), stop=end, skip_group_check=True)
                    last = nc.tensor.matmul(ps_o[:, 0:D], pT_lo[:, k % BANKS, b * P:(b + 1) * P], v[:, blk, 0, :],
                                            start=False, stop=end, skip_group_check=True)
                last.then_inc(pv_done, 1)

            pe.wait_ge(ident_done, 1)
            pe.wait_ge(w_in, 16)
            nc.tensor.transpose(ps_o[:, 0:D], w[:, :], ident[:, :]).then_inc(w_turned, 1)
            for k in range(TURNS + 2):
                if k < TURNS:
                    if k % PART_TURNS == 0:
                        pe.wait_ge(nodes_in[k // PART_TURNS], 16)
                    if k >= 2:
                        pe.wait_ge(nodesT_done, k - 1)
                    for b in range(PER_TURN):
                        last = nc.tensor.transpose(nodes_bank[k % 2][:, b * P:(b + 1) * P],
                                                   nodes_raw[:, k * PER_TURN + b, :], ident[:, :])
                    last.then_inc(nodes_turned, 1)
                y = k - 1
                if 0 <= y < TURNS:
                    pe.wait_ge(nodesT_done, y + 1)
                    if y == 0:
                        pe.wait_ge(wT_done, 1)
                    if y >= 2:
                        pe.wait_ge(y_lo_done, y - 1)
                    nc.tensor.matmul(y_bank[y % 2][:, :], wT[:, :], nodesT[:, y % 2, :], start=True, stop=True)\
                        .then_inc(y_made, 1)
                if k == 1:
                    for u in range(2):
                        turn_h(u, u, ps_s[u])
                if k >= 3 and k % 2 == 1:
                    j = (k - 3) // 2
                    if j == 0:
                        pe.wait_ge(hT_lo_done, 1)
                    pe.wait_ge(y_lo_done, 2 * (j + 1))
                    pe.wait_ge(taken, j + 1)
                    scores(0, j, ps_s[j % 2])

            def step(t, par, at):
                nxt = 1 - par

                def next_scores(j):
                    pe.wait_ge(taken, score_no(t + 1, j) - 1)
                    scores(nxt, j, score_area(nxt, j))

                def first_scores(u, s):
                    pe.wait_ge(taken, score_no(u, 0) - 1)
                    pe.wait_ge(hT_lo_done, u + 1)
                    scores(s, 0, score_area(s, 0))

                def next_turn(k):
                    if k % PER_EXP == 0:
                        pe.wait_ge(exp_done, t * SCORES + (k // PER_EXP + 1))
                    if at != 0 or k >= BANKS:
                        pe.wait_ge(turn_freed, turn_no(t, k) + 1 - BANKS)
                    turn(t, par, k)

                if at == 0:
                    first_scores(1, 1)
                    next_scores(1)
                for k in range(AHEAD):
                    next_turn(k)
                for k in range(TURNS):
                    if k + AHEAD < TURNS:
                        next_turn(k + AHEAD)
                    if k in S_AT and has(at, 1) and not (at == 0 and S_AT[k] == 1):
                        next_scores(S_AT[k])
                    if k == H_AT and has(at, 2):
                        pe.wait_ge(taken, h_no(t + 2) - 1)
                        turn_h(t + 2, par, h_area(par))
                    if k == 0 and at != 0:
                        pe.wait_ge(fin_done, t)
                    if k == TURNS - 1 and has(at, 2):
                        first_scores(t + 2, par)
                    pe.wait_ge(turn_freed, turn_no(t, k) + 1)
                    if at == 0 and k % PART_TURNS == 0:
                        pe.wait_ge(v_lo_done, k // PART_TURNS + 1)
                    product(k)

            steps(pe, step)


_INS = ["x", "adj", "L0_gnn_input", "L0_gnn_weight"]


def kernel(**inputs):
    import numpy as _np
    import concourse.bacc as _bacc
    from concourse import mybir as _mybir
    from concourse.bass_utils import run_bass_kernel_spmd as _run

    nc = _bacc.Bacc("TRN2", target_bir_lowering=False, num_devices=1)
    arrays, args = {}, []
    for name in _INS:
        a = _np.ascontiguousarray(inputs[name])
        arrays[f"in_{name}_dram"] = a
        args.append(nc.dram_tensor(f"in_{name}_dram", a.shape, _mybir.dt.from_np(a.dtype), kind="ExternalInput").ap())
    shape = inputs["x"].shape
    args.append(nc.dram_tensor("out_0_dram", shape, _mybir.dt.float32, kind="ExternalOutput").ap())
    gnn_masked_attention_kernel(nc, *args)
    r = _run(nc, [arrays], core_ids=[0])
    return r.results[0]["out_0_dram"]
```
